# Optimizing a Trainium2 kernel written in Bass

```python
import numpy as np
import jax
import jax.numpy as jnp

def _softmax(x, axis=-1):
    return jax.nn.softmax(x, axis=axis)

def _gelu(x):
    return jax.nn.gelu(x, approximate=True)

def _silu(x):
    return jax.nn.silu(x)

def _sigmoid(x):
    return jax.nn.sigmoid(x)

def _layernorm(x, axis=-1, eps=1e-05):
    m = jnp.mean(x, axis=axis, keepdims=True)
    v = jnp.var(x, axis=axis, keepdims=True)
    return (x - m) / jnp.sqrt(v + eps)

def _scatter_add(tgt, idx, src, axis=0):
    return tgt.at[idx].add(src)

def _segment_sum(src, seg, n):
    return jax.ops.segment_sum(src, seg, n)
kernel_name = 'mk_gnn_preln_d1_gnn_r8_ce9d1a'

def setup_inputs(seed: int=0):
    np.random.seed(seed)
    _w = jnp.asarray

    def _rec_inputs():
        import jax
        import jax.numpy as jnp
        _gk = jax.random.key(seed)
        x = -0.0006008 + 1.001 * jax.random.normal(jax.random.fold_in(_gk, 1), (12500, 128), jnp.float32)
        src = jax.random.randint(jax.random.fold_in(_gk, 2), (200000,), 0, 12500, jnp.int32)
        dst = jnp.minimum((12500 * jax.random.uniform(jax.random.fold_in(_gk, 3), (200000,)) ** 2.0).astype(jnp.int32), 99999)
        _o = jnp.argsort(dst, stable=True)
        src = src[_o]
        dst = dst[_o]
        edge_attr_64 = 0.000167468 + 1.0002 * jax.random.normal(jax.random.fold_in(_gk, 11), (200000, 64), jnp.float32)
        return (x, src, dst, edge_attr_64)
    x, src, dst, edge_attr_64 = _rec_inputs()

    def _L0_gnn_setup():
        import jax, jax.numpy as jnp
        import numpy as np
        N_NODES = 2500
        N_EDGES = 80000
        HIDDEN = 128
        EDGE_DIM = 64

        def _gru_cell(m, h, Wih, Whh, bih, bhh):
            gi = m @ Wih.T + bih
            gh = h @ Whh.T + bhh
            i_r, i_z, i_n = jnp.split(gi, 3, axis=-1)
            h_r, h_z, h_n = jnp.split(gh, 3, axis=-1)
            r = jax.nn.sigmoid(i_r + h_r)
            z = jax.nn.sigmoid(i_z + h_z)
            n = jnp.tanh(i_n + r * h_n)
            return (1.0 - z) * n + z * h

        def _dmpnn_layer(x, src, dst, edge_attr, W_msg, Wih, Whh, bih, bhh):
            n_nodes = x.shape[0]
            msg = jnp.concatenate([x[src], edge_attr], axis=-1) @ W_msg.T
            agg = jax.ops.segment_sum(msg, dst, num_segments=n_nodes)
            return _gru_cell(agg, x, Wih, Whh, bih, bhh)
        key = jax.random.key(seed)
        ks = jax.random.split(key, 16)
        s_h = 1.0 / np.sqrt(HIDDEN)
        s_m = 1.0 / np.sqrt(HIDDEN + EDGE_DIM)
        return {'x': jax.random.normal(ks[0], (N_NODES, HIDDEN), jnp.float32), 'edge_index': jax.random.randint(ks[1], (2, N_EDGES), 0, N_NODES, jnp.int64), 'edge_attr': jax.random.normal(ks[2], (N_EDGES, EDGE_DIM), jnp.float32), 'W_msg1': jax.random.normal(ks[3], (HIDDEN, HIDDEN + EDGE_DIM), jnp.float32) * s_m, 'Wih1': jax.random.normal(ks[4], (3 * HIDDEN, HIDDEN), jnp.float32) * s_h, 'Whh1': jax.random.normal(ks[5], (3 * HIDDEN, HIDDEN), jnp.float32) * s_h, 'bih1': jnp.zeros((3 * HIDDEN,), jnp.float32), 'bhh1': jnp.zeros((3 * HIDDEN,), jnp.float32), 'W_msg2': jax.random.normal(ks[6], (HIDDEN, HIDDEN + EDGE_DIM), jnp.float32) * s_m, 'Wih2': jax.random.normal(ks[7], (3 * HIDDEN, HIDDEN), jnp.float32) * s_h, 'Whh2': jax.random.normal(ks[8], (3 * HIDDEN, HIDDEN), jnp.float32) * s_h, 'bih2': jnp.zeros((3 * HIDDEN,), jnp.float32), 'bhh2': jnp.zeros((3 * HIDDEN,), jnp.float32)}
    _L0_gnn_all = _L0_gnn_setup()
    _L0_gnn_in = {k: v for k, v in _L0_gnn_all.items() if k in ('W_msg1', 'Wih1', 'Whh1', 'bih1', 'bhh1', 'W_msg2', 'Wih2', 'Whh2', 'bih2', 'bhh2')}
    del _L0_gnn_all
    return {'x': x, 'src': src, 'dst': dst, 'edge_attr_64': edge_attr_64, 'L0_gnn_W_msg1': _L0_gnn_in['W_msg1'], 'L0_gnn_Wih1': _L0_gnn_in['Wih1'], 'L0_gnn_Whh1': _L0_gnn_in['Whh1'], 'L0_gnn_bih1': _L0_gnn_in['bih1'], 'L0_gnn_bhh1': _L0_gnn_in['bhh1'], 'L0_gnn_W_msg2': _L0_gnn_in['W_msg2'], 'L0_gnn_Wih2': _L0_gnn_in['Wih2'], 'L0_gnn_Whh2': _L0_gnn_in['Whh2'], 'L0_gnn_bih2': _L0_gnn_in['bih2'], 'L0_gnn_bhh2': _L0_gnn_in['bhh2']}

def reference(x, src, dst, edge_attr_64, L0_gnn_W_msg1, L0_gnn_Wih1, L0_gnn_Whh1, L0_gnn_bih1, L0_gnn_bhh1, L0_gnn_W_msg2, L0_gnn_Wih2, L0_gnn_Whh2, L0_gnn_bih2, L0_gnn_bhh2):
    import jax
    import jax.numpy as jnp

    def _L0_gnn_ref(x, edge_index, edge_attr, W_msg1, Wih1, Whh1, bih1, bhh1, W_msg2, Wih2, Whh2, bih2, bhh2):
        import jax, jax.numpy as jnp
        import numpy as np
        N_NODES = 2500
        N_EDGES = 80000
        HIDDEN = 128
        EDGE_DIM = 64

        def _gru_cell(m, h, Wih, Whh, bih, bhh):
            gi = m @ Wih.T + bih
            gh = h @ Whh.T + bhh
            i_r, i_z, i_n = jnp.split(gi, 3, axis=-1)
            h_r, h_z, h_n = jnp.split(gh, 3, axis=-1)
            r = jax.nn.sigmoid(i_r + h_r)
            z = jax.nn.sigmoid(i_z + h_z)
            n = jnp.tanh(i_n + r * h_n)
            return (1.0 - z) * n + z * h

        def _dmpnn_layer(x, src, dst, edge_attr, W_msg, Wih, Whh, bih, bhh):
            n_nodes = x.shape[0]
            msg = jnp.concatenate([x[src], edge_attr], axis=-1) @ W_msg.T
            agg = jax.ops.segment_sum(msg, dst, num_segments=n_nodes)
            return _gru_cell(agg, x, Wih, Whh, bih, bhh)
        src, dst = (edge_index[0], edge_index[1])
        x = _dmpnn_layer(x, src, dst, edge_attr, W_msg1, Wih1, Whh1, bih1, bhh1)
        x = _dmpnn_layer(x, src, dst, edge_attr, W_msg2, Wih2, Whh2, bih2, bhh2)
        return x
    edge_index = jnp.stack([src, dst])
    h = jnp.maximum(_layernorm(x, axis=-1), 0.0)
    x = x + _L0_gnn_ref(h, edge_index, edge_attr_64, L0_gnn_W_msg1, L0_gnn_Wih1, L0_gnn_Whh1, L0_gnn_bih1, L0_gnn_bhh1, L0_gnn_W_msg2, L0_gnn_Wih2, L0_gnn_Whh2, L0_gnn_bih2, L0_gnn_bhh2)
    return x

_drawn_inputs = setup_inputs


def setup_inputs(seed=0):
    import zlib

    import numpy as np

    out = dict(_drawn_inputs(seed))
    spreads = {'L0_gnn_bih1': (0.0, 0.1),
     'L0_gnn_bhh1': (0.0, 0.352),
     'L0_gnn_bih2': (0.0, 0.426),
     'L0_gnn_bhh2': (0.0, 0.614)}
    factors = {}
    for name, (base, spread) in spreads.items():
        noise = np.random.default_rng([zlib.crc32(name.encode()), seed]).standard_normal(out[name].shape)
        drawn = base * np.exp(spread * noise) if base else spread * noise
        out[name] = jnp.asarray(drawn.astype(out[name].dtype))
    for name, factor in factors.items():
        out[name] = (out[name] * factor).astype(out[name].dtype)
    return out
```

```python
from contextlib import ExitStack

import concourse.bass as bass
from concourse import mybir

F32 = mybir.dt.float32
I32 = mybir.dt.int32
U32 = mybir.dt.uint32
ALU = mybir.AluOpType
ACT = mybir.ActivationFunctionType
AX = mybir.AxisListType

P = 128
TILES = 4
RING = 6
WIN = 80
XWIN = 128
XSHIFT = 7
CHUNK = 500
QUART = 125
NQ = CHUNK // QUART
EPS = 1e-5


def build(nc, x, src, dst, edge_attr, weights, h_table, x1_table, out):
    N, H = x.shape
    E, D = edge_attr.shape
    GROUP = P * TILES
    FULL = E // GROUP
    REST = (E - FULL * GROUP) // TILES
    GROUPS = FULL + 1
    BATCHES = FULL // RING
    CHUNKS = N // CHUNK
    assert FULL == BATCHES * RING and 0 < REST < P and E == FULL * GROUP + REST * TILES
    assert N == CHUNKS * CHUNK and H == P
    COLS = N + 300
    SROWS = 98
    SCOLS = 4
    NSTAT = SROWS * SCOLS
    assert NSTAT >= GROUPS and NSTAT - GROUPS < SROWS
    LNB = 5
    LT = LNB * NQ

    ctx = ExitStack()
    with ctx:
        def sb(name, shape, dt=F32):
            return ctx.enter_context(nc.sbuf_tensor(name, shape, dt))

        def sem(name):
            return ctx.enter_context(nc.semaphore(name))

        hT = sb("hT", [P, N])
        aggT = sb("aggT", [P, COLS])
        edgeT = sb("edgeT", [P, COLS])
        dst_rel = sb("dst_rel", [P, GROUPS, TILES])
        base_all = sb("base_all", [P, NSTAT])
        base_i = sb("base_i", [1, NSTAT], I32)
        extra_i = sb("extra_i", [1, NSTAT], I32)
        ready_i = sb("ready_i", [1, BATCHES + 1], I32)
        idx = sb("idx", [P, RING, TILES], I32)
        dst_in = sb("dst_in", [P, RING, TILES], I32)
        rows = sb("rows", [P, RING, TILES, H])
        attr = sb("attr", [P, RING, TILES, D])
        onehot = sb("onehot", [P, 2, TILES, WIN])
        onehot_x = sb("onehot_x", [P, TILES, XWIN])
        rel_x = sb("rel_x", [P, TILES])
        taken = [0]

        def start_only(parts, n, dt=F32):
            at = taken[0]
            taken[0] += n
            assert taken[0] <= COLS
            part = edgeT[0:parts, at:at + n]
            return part if dt == F32 else part.bitcast(dt)

        w_raw = start_only(P, 2 * 8 * P).rearrange("p (l k m) -> p l k m", l=2, k=8)
        wT = sb("wT", [P, 2, 8, P])
        b_raw = start_only(12, P)
        bT = sb("bT", [P, 12])
        b_gate = sb("b_gate", [P, 2, 2])
        ident = sb("ident", [P, P])
        lane_i = start_only(P, XWIN, I32)
        lane = sb("lane", [P, XWIN])
        zero = sb("zero", [P, 1])
        eps = sb("eps", [P, 1])
        ones = sb("ones", [P, 1])
        dst_rows = start_only(SROWS, SCOLS * GROUP, I32).rearrange("p (k e) -> p k e", k=SCOLS)
        stat = sb("stat", [SROWS, 2, SCOLS])
        stat_b = start_only(SROWS, 2 * SCOLS * P).rearrange("p (w k m) -> p w k m", w=2, k=SCOLS)
        max_all = start_only(P, NSTAT)
        gidx_i = start_only(P, NSTAT, I32)
        gidx = start_only(P, NSTAT)
        cend_i = sb("cend_i", [P, 1], I32)
        cend = sb("cend", [P, 1])
        need = sb("need", [P, 1])
        bend_i = start_only(P, BATCHES, I32)
        bend = start_only(P, BATCHES)
        span_i = start_only(1, NSTAT, I32)
        x_ln = aggT[0:QUART, :].rearrange("p (t f) -> p t f", f=H)
        bn = sb("bn", [QUART, LT, 6])
        mv = sb("mv", [QUART, LT, 2])
        std = sb("std", [QUART, LT])
        rstd = sb("rstd", [QUART, LT])
        h_ln = start_only(QUART, LNB * NQ * H).rearrange("p (k q f) -> p k q f", k=LNB, q=NQ)
        m_sb = sb("m_sb", [P, CHUNK])
        r_sb = sb("r_sb", [P, CHUNK])
        z_sb = sb("z_sb", [P, CHUNK])
        t_sb = r_sb
        n_sb = sb("n_sb", [P, CHUNK])
        h_new = sb("h_new", [P, CHUNK])
        x_in = sb("x_in", [QUART, NQ, H])
        out_sb = sb("out_sb", [QUART, NQ, H])

        ps_win = [ctx.enter_context(nc.psum_tensor(f"ps_win{i}", [P, 512], F32)) for i in range(2)]
        ps_m = ctx.enter_context(nc.psum_tensor("ps_m", [P, 512], F32))
        ps_r = ctx.enter_context(nc.psum_tensor("ps_r", [P, 512], F32))
        ps_z = ctx.enter_context(nc.psum_tensor("ps_z", [P, 512], F32))
        ps_ni = ctx.enter_context(nc.psum_tensor("ps_ni", [P, 512], F32))
        ps_nh = ctx.enter_context(nc.psum_tensor("ps_nh", [P, 512], F32))
        ps_t = ctx.enter_context(nc.psum_tensor("ps_t", [P, 512], F32))

        idx_loaded = [sem(f"idx_loaded{s}") for s in range(RING)]
        attr_loaded = [sem(f"attr_loaded{s}") for s in range(RING)]
        rows_loaded = [sem(f"rows_loaded{s}") for s in range(RING)]
        gather_issued = sem("gather_issued")
        dst_rows_loaded = sem("dst_rows_loaded")
        w_loaded = sem("w_loaded")
        x_loaded = [sem(f"x_loaded{i}") for i in range(CHUNKS // LNB)]
        consts_made = sem("consts_made")
        ident_zeroed = sem("ident_zeroed")
        prep = sem("prep")
        stat_ready = sem("stat_ready")
        base_ps_ready = sem("base_ps_ready")
        need_ready = sem("need_ready")
        ready_ps_ready = sem("ready_ps_ready")
        tables_ready = sem("tables_ready")
        w_turned = sem("w_turned")
        w_kept = sem("w_kept")
        b_turned = sem("b_turned")
        bias_ready = sem("bias_ready")
        ln_stats = sem("ln_stats")
        ln_aggr = sem("ln_aggr")
        ln_std = sem("ln_std")
        ln_rstd = sem("ln_rstd")
        ln_norm = sem("ln_norm")
        ln_relu = sem("ln_relu")
        ln_turned = sem("ln_turned")
        ln_kept = sem("ln_kept")
        h_stored = sem("h_stored")
        sums_zeroed = sem("sums_zeroed")
        rel_ready = sem("rel_ready")
        onehot_ready = sem("onehot_ready")
        group_summed = sem("group_summed")
        window_added = sem("window_added")
        rel_x_ready = sem("rel_x_ready")
        x_onehot_ready = sem("x_onehot_ready")
        x_summed = sem("x_summed")
        x_added = sem("x_added")
        msg_ready = sem("msg_ready")
        m_kept = sem("m_kept")
        r_summed = sem("r_summed")
        n_summed = sem("n_summed")
        z_summed = sem("z_summed")
        r_ready = sem("r_ready")
        z_ready = sem("z_ready")
        t_scaled = sem("t_scaled")
        t_ready = sem("t_ready")
        n_ready = sem("n_ready")
        d_ready = sem("d_ready")
        dz_ready = sem("dz_ready")
        h_ready = sem("h_ready")
        h_turned = sem("h_turned")
        hT_kept = sem("hT_kept")
        agg_cleared = sem("agg_cleared")
        x_in_loaded = sem("x_in_loaded")
        out_ready = sem("out_ready")
        out_stored = sem("out_stored")
        chunk_done = sem("chunk_done")

        def slot_use(layer, b, s):
            return layer * (BATCHES + (s == 0)) + b

        def each_group(eng, layer, group, after_batch=None):
            for s in range(RING):
                group(0, s, s, P, s)
            if after_batch:
                after_batch(0)
            with eng.Fori(1, BATCHES) as b:
                for s in range(RING):
                    group(b, s, b * RING + s, P, None)
                if after_batch:
                    after_batch(b)
            group(BATCHES, 0, FULL, REST, None)

        def ready_chunks(eng, b, chunk):
            lo = eng.value_load(ready_i[0:1, bass.ds(b, 1)], min_val=0, max_val=CHUNKS)
            hi = eng.value_load(ready_i[0:1, bass.ds(b + 1, 1)], min_val=0, max_val=CHUNKS)
            with eng.If(lo < hi):
                with eng.Fori(lo, hi) as c:
                    chunk(c)

        def last_chunks(eng, chunk):
            lo = eng.value_load(ready_i[0:1, BATCHES:BATCHES + 1], min_val=0, max_val=CHUNKS)
            with eng.If(lo < CHUNKS):
                with eng.Fori(lo, CHUNKS) as c:
                    chunk(c)

        def edges(a, g, parts):
            w = a.shape[1] if len(a.shape) == 2 else 1
            flat = a if w == 1 else a.rearrange("e d -> (e d)")
            if parts == P:
                v = flat[0:FULL * GROUP * w].rearrange("(g p j) -> g p j", g=FULL, p=P)
                return v[bass.ds(g, 1), :, :].rearrange("o p j -> p (o j)")
            return flat[FULL * GROUP * w:E * w].rearrange("(p j) -> p j", p=parts)

        def nodes(a, c):
            v = a.rearrange("(c q p) f -> c p q f", q=NQ, p=QUART)
            return v[bass.ds(c, 1), :, :, :].rearrange("o p q f -> p (o q) f")

        def cols(t, c):
            return t[:, bass.ds(c * CHUNK, CHUNK)]

        ctx.enter_context(nc.allow_non_contiguous_dma("edge groups are 16 bytes to a partition"))
        block = ctx.enter_context(nc.Block())

        @block.sync
        def _(sp):
            head = (SCOLS - 1) * SROWS * GROUP
            sp.dma_start(dst_rows[:, 0:SCOLS - 1, :],
                         dst[0:head].rearrange("(k p j) -> p k j", p=SROWS, j=GROUP)).then_inc(dst_rows_loaded, 16)
            more = FULL - (SCOLS - 1) * SROWS
            sp.dma_start(dst_rows[0:more, SCOLS - 1, :],
                         dst[head:FULL * GROUP].rearrange("(p j) -> p j", j=GROUP)).then_inc(dst_rows_loaded, 16)
            for p in range(more, SROWS):
                sp.dma_start(dst_rows[p:p + 1, SCOLS - 1, :],
                             dst[E - GROUP:E].rearrange("(o j) -> o j", o=1)).then_inc(dst_rows_loaded, 16)
            xv = x.rearrange("(i t p) f -> i p t f", t=LT, p=QUART)
            for i in range(CHUNKS // LNB):
                sp.dma_start(x_ln[:, i * LT:(i + 1) * LT, :], xv[i]).then_inc(x_loaded[i], 16)
            for layer in range(2):
                w_msg, w_ih, w_hh, b_ih, b_hh = weights[layer]
                sp.dma_start(w_raw[:, layer, 0, :], w_msg[:, 0:H]).then_inc(w_loaded, 16)
                sp.dma_start(w_raw[:, layer, 1, 0:D], w_msg[:, H:H + D]).then_inc(w_loaded, 16)
                sp.dma_start(w_raw[:, layer, 2:5, :], w_ih.rearrange("(t p) k -> p t k", p=P)).then_inc(w_loaded, 16)
                sp.dma_start(w_raw[:, layer, 5:8, :], w_hh.rearrange("(t p) k -> p t k", p=P)).then_inc(w_loaded, 16)
                for k, b in enumerate((b_ih, b_hh)):
                    o = 6 * layer + 3 * k
                    sp.dma_start(b_raw[o:o + 3, :], b.rearrange("(t p) -> t p", p=P)).then_inc(w_loaded, 16)

            for layer in range(2):
                def group(b, s, g, parts, first):
                    again = layer or first is None
                    if again:
                        sp.wait_ge(rows_loaded[s], slot_use(layer, b, s) * 16 * TILES)
                    sp.dma_start(idx[0:parts, s, :], edges(src, g, parts)).then_inc(idx_loaded[s], 16)
                    if layer == 0:
                        if again:
                            sp.wait_ge(group_summed, g - RING + 1)
                        sp.dma_start(dst_in[0:parts, s, :], edges(dst, g, parts)).then_inc(attr_loaded[s], 16)
                        sp.dma_start(attr[0:parts, s, :, :].rearrange("p j d -> p (j d)"),
                                     edges(edge_attr, g, parts)).then_inc(attr_loaded[s], 16)

                each_group(sp, layer, group)

        @block.gpsimd
        def _(pool):
            nc.gpsimd.memset(ident[:, :], 0.0).then_inc(ident_zeroed, 1)
            nc.gpsimd.iota(lane_i[:, :], pattern=[[1, XWIN]], base=0, channel_multiplier=0)
            nc.gpsimd.iota(gidx_i[:, :], pattern=[[1, NSTAT]], base=1, channel_multiplier=0)
            nc.gpsimd.iota(cend_i[:, :], pattern=[[1, 1]], base=CHUNK, channel_multiplier=CHUNK)
            nc.gpsimd.iota(bend_i[:, :], pattern=[[RING, BATCHES]], base=RING, channel_multiplier=0)
            nc.gpsimd.memset(zero[:, :], 0.0)
            nc.gpsimd.memset(eps[:, :], EPS)
            nc.gpsimd.memset(ones[:, :], 1.0)
            pool.wait_ge(ident_zeroed, 1)
            nc.gpsimd.affine_select(out=ident[:, :], in_=ident[:, :], compare_op=ALU.not_equal, fill=1.0, base=0,
                                    pattern=[[-1, P]], channel_multiplier=1).then_inc(consts_made, 1)

            for layer in range(2):
                table = (h_table, x1_table)[layer]
                if layer == 0:
                    pool.wait_ge(h_stored, 16 * CHUNKS)
                else:
                    pool.wait_ge(out_stored, 16 * CHUNKS)

                def group(b, s, g, parts, first):
                    if layer or first is None:
                        pool.wait_ge(group_summed, layer * GROUPS + g - RING + 1)
                    pool.wait_ge(idx_loaded[s], 16 * (slot_use(layer, b, s) + 1))
                    pool.sem_inc(gather_issued, 1)
                    for j in range(TILES):
                        nc.gpsimd.indirect_dma_start(
                            out=rows[0:parts, s, j, :], out_offset=None, in_=table[:, :],
                            in_offset=bass.IndirectOffsetOnAxis(ap=idx[0:parts, s, j:j + 1].bitcast(U32), axis=0),
                        ).then_inc(rows_loaded[s], 16)

                each_group(pool, layer, group)

        @block.tensor
        def _(pe):
            pe.wait_ge(consts_made, 1)
            pe.wait_ge(stat_ready, 1)
            for w, ps in ((0, ps_r), (1, ps_z)):
                for k in range(SCOLS):
                    mm = nc.tensor.matmul(ps[:, k * SROWS:(k + 1) * SROWS], stat_b[:, w, k, :],
                                          ident[0:SROWS, 0:SROWS], start=True, stop=True)
            mm.then_inc(base_ps_ready, 1)
            pe.wait_ge(need_ready, 1)
            nc.tensor.matmul(ps_m[0:1, 0:BATCHES], ones[0:CHUNKS, :], bend[0:CHUNKS, :],
                             start=True, stop=True).then_inc(ready_ps_ready, 1)
            pe.wait_ge(w_loaded, 16 * 12)
            nc.tensor.transpose(ps_ni[:, 0:12], b_raw[:, :], ident[0:12, 0:12]).then_inc(b_turned, 1)
            for layer in range(2):
                for k in range(8):
                    i = layer * 8 + k
                    bank = (ps_win[0], ps_win[1])[i % 2]
                    if i >= 2:
                        pe.wait_ge(w_kept, i - 1)
                    if k == 1:
                        nc.tensor.transpose(bank[0:D, 0:P], w_raw[:, layer, k, 0:D], ident[:, :]).then_inc(w_turned, 1)
                    else:
                        nc.tensor.transpose(bank[:, 0:P], w_raw[:, layer, k, :], ident[:, :]).then_inc(w_turned, 1)
            with pe.Fori(0, CHUNKS // LNB) as i:
                for k in range(LNB):
                    pe.wait_ge(ln_relu, i * LNB + k + 1)
                    pe.wait_ge(ln_kept, i * LNB + k + 1)
                    for q in range(NQ):
                        tr = nc.tensor.transpose(ps_t[:, q * QUART:(q + 1) * QUART], h_ln[:, k, q, :],
                                                 ident[0:QUART, 0:QUART])
                    tr.then_inc(ln_turned, 1)

            pe.wait_ge(tables_ready, 1)
            pe.wait_ge(ln_kept, CHUNKS + 1)
            extra_count = pe.alloc_register("pe_extra_count")
            pe.reg_mov(extra_count, 0)

            for layer in range(2):
                def group(b, s, g, parts, first):
                    gg = layer * GROUPS + g
                    bank = ps_win[s % 2]
                    pe.wait_ge(rows_loaded[s], 16 * TILES * (slot_use(layer, b, s) + 1))
                    if layer == 0:
                        pe.wait_ge(attr_loaded[s], 32 * (slot_use(0, b, s) + 1))
                    pe.wait_ge(onehot_ready, gg + 1)
                    if layer or first is None or first >= 2:
                        pe.wait_ge(window_added, gg - 1)
                    elif first is not None and first == 0:
                        pe.wait_ge(w_kept, 16)
                    n = pe.value_load(extra_i[0:1, bass.ds(g, 1)], min_val=0, max_val=N)
                    with pe.If(n > 0):
                        with pe.Fori(0, n):
                            pe.reg_add(extra_count, extra_count, 1)
                            count = pe.snap(extra_count, min_val=1, max_val=1 << 20)
                            pe.wait_ge(x_onehot_ready, count)
                            for j in range(TILES):
                                mm = nc.tensor.matmul(bank[:, 0:XWIN], rows[0:parts, s, j, :],
                                                      onehot_x[0:parts, j, :], start=(j == 0), stop=(j == TILES - 1))
                            if layer == 0:
                                for j in range(TILES):
                                    mm = nc.tensor.matmul(bank[0:D, XWIN:2 * XWIN], attr[0:parts, s, j, :],
                                                          onehot_x[0:parts, j, :],
                                                          start=(j == 0), stop=(j == TILES - 1))
                            mm.then_inc(x_summed, 1)
                            pe.wait_ge(x_added, count)
                    if layer == 0:
                        for j in range(TILES):
                            nc.tensor.matmul(bank[0:D, WIN:2 * WIN], attr[0:parts, s, j, :],
                                             onehot[0:parts, s % 2, j, :], start=(j == 0), stop=(j == TILES - 1))
                    for j in range(TILES):
                        mm = nc.tensor.matmul(bank[:, 0:WIN], rows[0:parts, s, j, :],
                                              onehot[0:parts, s % 2, j, :], start=(j == 0), stop=(j == TILES - 1))
                    mm.then_inc(group_summed, 1)

                def chunk(c):
                    cc = layer * CHUNKS + c
                    pe.wait_ge(chunk_done, cc + 1)
                    nc.tensor.matmul(ps_m[:, 0:CHUNK], wT[:, layer, 0, :], cols(aggT, c), start=True, stop=False)
                    nc.tensor.matmul(ps_m[:, 0:CHUNK], wT[0:D, layer, 1, :], cols(edgeT[0:D, :], c),
                                     start=False, stop=True).then_inc(msg_ready, 1)
                    nc.tensor.matmul(ps_nh[:, 0:CHUNK], wT[:, layer, 7, :], cols(hT, c), start=True, stop=True)
                    nc.tensor.matmul(ps_r[:, 0:CHUNK], wT[:, layer, 5, :], cols(hT, c), start=True, stop=False)
                    nc.tensor.matmul(ps_z[:, 0:CHUNK], wT[:, layer, 6, :], cols(hT, c), start=True, stop=False)
                    pe.wait_ge(m_kept, cc + 1)
                    nc.tensor.matmul(ps_r[:, 0:CHUNK], wT[:, layer, 2, :], m_sb[:, :],
                                     start=False, stop=True).then_inc(r_summed, 1)
                    nc.tensor.matmul(ps_ni[:, 0:CHUNK], wT[:, layer, 4, :], m_sb[:, :],
                                     start=True, stop=True).then_inc(n_summed, 1)
                    nc.tensor.matmul(ps_z[:, 0:CHUNK], wT[:, layer, 3, :], m_sb[:, :],
                                     start=False, stop=True).then_inc(z_summed, 1)
                    pe.wait_ge(h_ready, cc + 1)
                    for q in range(NQ):
                        tr = nc.tensor.transpose(ps_t[0:QUART, q * P:(q + 1) * P],
                                                 h_new[:, q * QUART:(q + 1) * QUART], ident[:, :])
                    tr.then_inc(h_turned, 1)

                def after_batch(b):
                    pe.wait_ge(window_added, layer * GROUPS + (b + 1) * RING)
                    ready_chunks(pe, b, chunk)

                if layer == 1:
                    pe.wait_ge(hT_kept, CHUNKS)
                each_group(pe, layer, group, after_batch)
                pe.wait_ge(window_added, (layer + 1) * GROUPS)
                last_chunks(pe, chunk)

        @block.vector
        def _(dve):
            step = [0]

            def chained(ins):
                step[0] += 1
                ins.then_inc(prep, 1)
                dve.wait_ge(prep, step[0])

            dve.wait_ge(dst_rows_loaded, 16 * (2 + SROWS - (FULL - (SCOLS - 1) * SROWS)))
            nc.vector.tensor_reduce(stat[:, 0, :], dst_rows[:, :, :], AX.X, ALU.min)
            chained(nc.vector.tensor_reduce(stat[:, 1, :], dst_rows[:, :, :], AX.X, ALU.max))
            chained(nc.vector.tensor_scalar(stat[:, :, :], stat[:, :, :], 0.0, float(N), ALU.max, ALU.min))
            nc.vector.tensor_copy(stat_b[:, :, :, :],
                                  stat[:, :, :].unsqueeze(3).to_broadcast([SROWS, 2, SCOLS, P])).then_inc(stat_ready, 1)
            dve.wait_ge(consts_made, 1)
            nc.vector.tensor_copy(lane[:, :], lane_i[:, :])
            nc.vector.tensor_copy(gidx[:, :], gidx_i[:, :])
            nc.vector.tensor_copy(cend[:, :], cend_i[:, :])
            nc.vector.tensor_copy(bend[:, :], bend_i[:, :])
            dve.wait_ge(base_ps_ready, 1)
            nc.vector.tensor_copy(base_all[:, :], ps_r[:, 0:NSTAT])
            chained(nc.vector.tensor_copy(max_all[:, :], ps_z[:, 0:NSTAT]))
            nc.vector.tensor_copy(base_i[:, :], base_all[0:1, :])
            chained(nc.vector.tensor_tensor(max_all[0:1, :], max_all[0:1, :], base_all[0:1, :], ALU.subtract))
            chained(nc.vector.tensor_scalar(span_i[:, :], max_all[0:1, :], float(XWIN - WIN), None, ALU.add))
            nc.vector.tensor_scalar(extra_i[:, :], span_i[:, :], XSHIFT, None, ALU.arith_shift_right)
            chained(nc.vector.scalar_tensor_tensor(out=gidx[:, :], in0=base_all[:, :], scalar=cend[:, 0:1],
                                                   in1=gidx[:, :], op0=ALU.is_lt, op1=ALU.mult))
            chained(nc.vector.tensor_reduce(need[:, :], gidx[:, :], AX.X, ALU.max))
            nc.vector.tensor_scalar(bend[:, :], bend[:, :], need[:, 0:1], None, ALU.is_ge).then_inc(need_ready, 1)
            nc.vector.memset(ready_i[0:1, 0:1], 0)
            dve.wait_ge(ready_ps_ready, 1)
            nc.vector.tensor_copy(ready_i[0:1, 1:BATCHES + 1], ps_m[0:1, 0:BATCHES]).then_inc(tables_ready, 1)

            dve.wait_ge(b_turned, 1)
            chained(nc.vector.tensor_copy(bT[:, :], ps_ni[:, 0:12]))
            for layer in range(2):
                o = 6 * layer
                ins = nc.vector.tensor_tensor(b_gate[:, layer, :], bT[:, o:o + 2], bT[:, o + 3:o + 5], ALU.add)
            ins.then_inc(bias_ready, 1)

            for i in range(CHUNKS // LNB):
                dve.wait_ge(x_loaded[i], 16)
                for t in range(LT):
                    ins = nc.vector.bn_stats(bn[:, t, :], x_ln[:, i * LT + t, :])
                ins.then_inc(ln_stats, 1)
                dve.wait_ge(ln_stats, i + 1)
                for t in range(LT):
                    ins = nc.vector.bn_aggr(mv[:, t, :], bn[:, t, :])
                ins.then_inc(ln_aggr, 1)
                dve.wait_ge(ln_std, i + 1)
                nc.vector.reciprocal(rstd[:, :], std[:, :]).then_inc(ln_rstd, 1)
                dve.wait_ge(ln_rstd, i + 1)
                for k in range(LNB):
                    for q in range(NQ):
                        t = k * NQ + q
                        xt = x_ln[:, i * LT + t, :]
                        ins = nc.vector.tensor_scalar(xt, xt, mv[:, t, 0:1], rstd[:, t:t + 1],
                                                      ALU.subtract, ALU.mult)
                    ins.then_inc(ln_norm, 1)
            dve.wait_ge(ln_relu, CHUNKS)
            dve.wait_ge(ln_turned, CHUNKS)
            dve.wait_ge(h_stored, 16 * CHUNKS)
            dve.wait_ge(w_turned, 16)
            nc.vector.memset(edgeT[:, :], 0.0)
            nc.vector.memset(aggT[:, :], 0.0).then_inc(sums_zeroed, 1)
            dve.wait_ge(sums_zeroed, 1)

            extra_count = dve.alloc_register("dve_extra_count")
            dve.reg_mov(extra_count, 0)

            for layer in range(2):
                def add_window(g, s, first, count_before):
                    gg = layer * GROUPS + g
                    base = dve.value_load(base_i[0:1, bass.ds(g, 1)], min_val=0, max_val=N)
                    dve.wait_ge(group_summed, gg + 1)
                    if layer or first is None or first >= 1:
                        dve.wait_ge(window_added, gg)
                    if layer == 0:
                        e = edgeT[0:D, bass.ds(base, WIN)]
                        nc.vector.tensor_tensor(e, e, ps_win[s % 2][0:D, WIN:2 * WIN], ALU.add)
                    a = aggT[:, bass.ds(base, WIN)]
                    nc.vector.tensor_tensor(a, a, ps_win[s % 2][:, 0:WIN], ALU.add).then_inc(window_added, 1)

                def onehot_of(b, s, g, parts, first):
                    gg = layer * GROUPS + g
                    rel = dst_rel[0:parts, bass.ds(g, 1), :].rearrange("p o j -> p (o j)")
                    if layer == 0:
                        dve.wait_ge(attr_loaded[s], 32 * (slot_use(0, b, s) + 1))
                        nc.vector.tensor_scalar(rel, dst_in[0:parts, s, :], float(N), base_all[0:parts, bass.ds(g, 1)],
                                                ALU.min, ALU.subtract).then_inc(rel_ready, 1)
                        dve.wait_ge(rel_ready, g + 1)
                    if layer or first is None or first >= 2:
                        dve.wait_ge(group_summed, gg - 1)
                    nc.vector.tensor_tensor(
                        onehot[0:parts, s % 2, :, :],
                        lane[0:parts, 0:WIN].unsqueeze(1).to_broadcast([parts, TILES, WIN]),
                        rel.unsqueeze(2).to_broadcast([parts, TILES, WIN]), ALU.is_equal).then_inc(onehot_ready, 1)
                    n = dve.value_load(extra_i[0:1, bass.ds(g, 1)], min_val=0, max_val=N)
                    with dve.If(n > 0):
                        base = dve.value_load(base_i[0:1, bass.ds(g, 1)], min_val=0, max_val=N)
                        nc.vector.tensor_scalar(rel_x[0:parts, :], rel, float(WIN), None,
                                                ALU.subtract).then_inc(rel_x_ready, 1)
                        with dve.Fori(0, n) as k:
                            dve.reg_add(extra_count, extra_count, 1)
                            count = dve.snap(extra_count, min_val=1, max_val=1 << 20)
                            dve.drain()
                            nc.vector.tensor_tensor(
                                onehot_x[0:parts, :, :],
                                lane[0:parts, :].unsqueeze(1).to_broadcast([parts, TILES, XWIN]),
                                rel_x[0:parts, :].unsqueeze(2).to_broadcast([parts, TILES, XWIN]),
                                ALU.is_equal).then_inc(x_onehot_ready, 1)
                            dve.wait_ge(x_summed, count)
                            nc.vector.tensor_scalar(rel_x[0:parts, :], rel_x[0:parts, :], float(XWIN), None,
                                                    ALU.subtract)
                            at = base + k * XWIN + WIN
                            at = nc.s_assert_within(at, WIN, COLS - XWIN,
                                                    skip_runtime_bounds_check_because="the last extra window starts at or before the group's greatest node")
                            if layer == 0:
                                e = edgeT[0:D, bass.ds(at, XWIN)]
                                nc.vector.tensor_tensor(e, e, ps_win[s % 2][0:D, XWIN:2 * XWIN], ALU.add)
                            a = aggT[:, bass.ds(at, XWIN)]
                            nc.vector.tensor_tensor(a, a, ps_win[s % 2][:, 0:XWIN], ALU.add).then_inc(x_added, 1)
                            dve.wait_ge(x_added, count)

                def group(b, s, g, parts, first):
                    onehot_of(b, s, g, parts, first)
                    if s > 0:
                        add_window(g - 1, s - 1, None if first is None else first - 1, 0)
                    if s == RING - 1 or parts < P:
                        add_window(g, s, first, 0)

                def chunk(c):
                    cc = layer * CHUNKS + c
                    o = 6 * layer
                    dve.wait_ge(n_summed, cc + 1)
                    dve.wait_ge(r_ready, cc + 1)
                    nc.vector.scalar_tensor_tensor(out=t_sb[:, :], in0=ps_nh[:, 0:CHUNK], scalar=bT[:, o + 5:o + 6],
                                                   in1=r_sb[:, :], op0=ALU.add, op1=ALU.mult).then_inc(t_scaled, 1)
                    dve.wait_ge(t_scaled, cc + 1)
                    nc.vector.tensor_tensor(t_sb[:, :], t_sb[:, :], ps_ni[:, 0:CHUNK], ALU.add).then_inc(t_ready, 1)
                    dve.wait_ge(n_ready, cc + 1)
                    nc.vector.tensor_tensor(t_sb[:, :], cols(hT, c), n_sb[:, :], ALU.subtract).then_inc(d_ready, 1)
                    dve.wait_ge(d_ready, cc + 1)
                    dve.wait_ge(z_ready, cc + 1)
                    nc.vector.tensor_tensor(t_sb[:, :], t_sb[:, :], z_sb[:, :], ALU.mult).then_inc(dz_ready, 1)
                    dve.wait_ge(dz_ready, cc + 1)
                    nc.vector.tensor_tensor(h_new[:, :], n_sb[:, :], t_sb[:, :], ALU.add).then_inc(h_ready, 1)
                    if layer == 1:
                        dve.wait_ge(h_turned, cc + 1)
                        dve.wait_ge(x_in_loaded, 16 * (c + 1))
                        nc.vector.tensor_tensor(
                            out_sb[:, :, :], x_in[:, :, :],
                            ps_t[0:QUART, 0:NQ * H].rearrange("p (q f) -> p q f", f=H), ALU.add).then_inc(out_ready, 1)

                def after_batch(b):
                    ready_chunks(dve, b, chunk)

                if layer == 1:
                    dve.wait_ge(agg_cleared, CHUNKS)
                each_group(dve, layer, group, after_batch)
                last_chunks(dve, chunk)

        @block.scalar
        def _(act):
            act.sem_inc(chunk_done, 1)
            act.sem_inc(ln_kept, 1)
            for i in range(16):
                layer, k = i // 8, i % 8
                part = D if k == 1 else P
                act.wait_ge(w_turned, i + 1)
                nc.scalar.copy(wT[0:part, layer, k, :], ps_win[i % 2][0:part, 0:P]).then_inc(w_kept, 1)

            act.wait_ge(consts_made, 1)
            for i in range(CHUNKS // LNB):
                act.wait_ge(ln_aggr, i + 1)
                nc.scalar.activation(std[:, :], mv[:, :, 1], ACT.Sqrt, bias=eps[0:QUART, :]).then_inc(ln_std, 1)
                for k in range(LNB):
                    c = i * LNB + k
                    act.wait_ge(ln_norm, c + 1)
                    if i:
                        act.wait_ge(h_stored, 16 * i * LNB)
                        act.wait_ge(ln_turned, (i - 1) * LNB + k + 1)
                    nc.scalar.activation(h_ln[:, k, :, :], x_ln[:, c * NQ:(c + 1) * NQ, :], ACT.Relu).then_inc(ln_relu, 1)
                    act.wait_ge(ln_relu, c + 1)
                    act.dma_start(nodes(h_table, c), h_ln[:, k, :, :]).then_inc(h_stored, 16)
                    act.wait_ge(ln_turned, c + 1)
                    nc.scalar.copy(hT[:, c * CHUNK:(c + 1) * CHUNK], ps_t[:, 0:CHUNK]).then_inc(ln_kept, 1)

            act.wait_ge(tables_ready, 1)
            act.wait_ge(bias_ready, 1)
            for layer in range(2):
                def chunk(c):
                    cc = layer * CHUNKS + c
                    o = 6 * layer
                    if layer == 1:
                        act.dma_start(x_in[:, :, :], nodes(x, c)).then_inc(x_in_loaded, 16)
                    act.wait_ge(msg_ready, cc + 1)
                    nc.scalar.copy(m_sb[:, :], ps_m[:, 0:CHUNK]).then_inc(m_kept, 1)
                    if layer == 0:
                        nc.scalar.copy(cols(aggT, c), zero[:, 0:1].to_broadcast([P, CHUNK])).then_inc(agg_cleared, 1)
                    act.wait_ge(r_summed, cc + 1)
                    nc.scalar.activation(r_sb[:, :], ps_r[:, 0:CHUNK], ACT.Sigmoid,
                                         bias=b_gate[:, layer, 0:1]).then_inc(r_ready, 1)
                    act.wait_ge(z_summed, cc + 1)
                    nc.scalar.activation(z_sb[:, :], ps_z[:, 0:CHUNK], ACT.Sigmoid,
                                         bias=b_gate[:, layer, 1:2]).then_inc(z_ready, 1)
                    act.wait_ge(t_ready, cc + 1)
                    nc.scalar.activation(n_sb[:, :], t_sb[:, :], ACT.Tanh, bias=bT[:, o + 2:o + 3]).then_inc(n_ready, 1)
                    act.wait_ge(h_ready, cc + 1)
                    if layer == 0:
                        nc.scalar.copy(cols(hT, c), h_new[:, :]).then_inc(hT_kept, 1)
                        act.wait_ge(h_turned, cc + 1)
                        nc.scalar.copy(out_sb[:, :, :].rearrange("p q f -> p (q f)"),
                                       ps_t[0:QUART, 0:NQ * H]).then_inc(out_ready, 1)
                    act.wait_ge(out_ready, cc + 1)
                    act.dma_start(nodes((x1_table, out)[layer], c), out_sb[:, :, :]).then_inc(out_stored, 16)
                    act.wait_ge(out_stored, 16 * (cc + 1))
                    act.sem_inc(chunk_done, 1)

                for b in [0]:
                    ready_chunks(act, 0, chunk)
                with act.Fori(1, BATCHES) as b:
                    ready_chunks(act, b, chunk)
                last_chunks(act, chunk)


_WEIGHTS = ["W_msg", "Wih", "Whh", "bih", "bhh"]


def kernel(**inputs):
    import numpy as _np
    import concourse.bacc as _bacc
    from concourse import mybir as _mybir
    from concourse.bass_utils import run_bass_kernel_spmd as _run

    nc = _bacc.Bacc("TRN2", target_bir_lowering=False, num_devices=1)
    arrays, aps = {}, {}
    names = ["x", "src", "dst", "edge_attr_64"] + [f"L0_gnn_{w}{n}" for n in (1, 2) for w in _WEIGHTS]
    for name in names:
        a = _np.ascontiguousarray(inputs[name])
        arrays[f"in_{name}_dram"] = a
        aps[name] = nc.dram_tensor(f"in_{name}_dram", a.shape, _mybir.dt.from_np(a.dtype), kind="ExternalInput").ap()
    shape = arrays["in_x_dram"].shape
    h_table = nc.dram_tensor("h_table", shape, F32, kind="Internal").ap()
    x1_table = nc.dram_tensor("x1_table", shape, F32, kind="Internal").ap()
    out = nc.dram_tensor("out_dram", shape, F32, kind="ExternalOutput").ap()
    weights = [[aps[f"L0_gnn_{w}{n}"] for w in _WEIGHTS] for n in (1, 2)]
    build(nc, aps["x"], aps["src"], aps["dst"], aps["edge_attr_64"], weights, h_table, x1_table, out)
    r = _run(nc, [arrays], core_ids=[0])
    return r.results[0]["out_dram"]
```

```python
from contextlib import ExitStack

import concourse.bass as bass
from concourse import mybir

F32 = mybir.dt.float32
I32 = mybir.dt.int32
U32 = mybir.dt.uint32
ALU = mybir.AluOpType
ACT = mybir.ActivationFunctionType
AX = mybir.AxisListType

P = 128
TILES = 4
RING = 6
WIN = 80
XWIN = 128
XSHIFT = 7
XAT = 256
CHUNK = 500
QUART = 125
NQ = CHUNK // QUART
X_LOADS = (1, 2, 2, 5, 5, 5, 5)
EPS = 1e-5


def build(nc, x, src, dst, edge_attr, weights, h_table, x1_table, out):
    N, H = x.shape
    E, D = edge_attr.shape
    GROUP = P * TILES
    FULL = E // GROUP
    REST = (E - FULL * GROUP) // TILES
    GROUPS = FULL + 1
    BATCHES = FULL // RING
    CHUNKS = N // CHUNK
    assert FULL == BATCHES * RING and 0 < REST < P and E == FULL * GROUP + REST * TILES
    assert N == CHUNKS * CHUNK and H == P and sum(X_LOADS) == CHUNKS
    x_starts = [sum(X_LOADS[:i]) for i in range(len(X_LOADS))]
    COLS = N + 300
    SROWS = 98
    SCOLS = 4
    NSTAT = SROWS * SCOLS
    assert NSTAT >= GROUPS and NSTAT - GROUPS < SROWS

    ctx = ExitStack()
    with ctx:
        def sb(name, shape, dt=F32):
            return ctx.enter_context(nc.sbuf_tensor(name, shape, dt))

        def sem(name):
            return ctx.enter_context(nc.semaphore(name))

        hT = sb("hT", [P, N])
        aggT = sb("aggT", [P, COLS])
        edgeT = sb("edgeT", [P, COLS])
        dst_rel = sb("dst_rel", [P, GROUPS, TILES])
        base_all = sb("base_all", [P, NSTAT])
        base_i = sb("base_i", [1, NSTAT], I32)
        extra_i = sb("extra_i", [1, NSTAT], I32)
        ready_i = sb("ready_i", [1, BATCHES + 1], I32)
        idx = sb("idx", [P, RING, TILES], I32)
        dst_in = sb("dst_in", [P, RING, TILES], I32)
        rows = sb("rows", [P, RING, TILES, H])
        attr = sb("attr", [P, RING, TILES, D])
        onehot = sb("onehot", [P, 2, TILES, WIN])
        onehot_x = sb("onehot_x", [P, TILES, XWIN])
        rel_x = sb("rel_x", [P, TILES])
        room = [N]

        def start_only(parts, n, dt=F32):
            room[0] -= n
            part = hT[0:parts, room[0]:room[0] + n]
            return part if dt == F32 else part.bitcast(dt)

        gru = sb("gru", [P, 5 * CHUNK])
        w_raw = gru[:, 0:2 * 8 * P].rearrange("p (l k m) -> p l k m", l=2, k=8)
        wT = sb("wT", [P, 2, 8, P])
        b_raw = start_only(12, P)
        bT = sb("bT", [P, 12])
        b_gate = sb("b_gate", [P, 2, 2])
        ident = sb("ident", [P, P])
        lane = sb("lane", [P, XWIN])
        zero = sb("zero", [P, 1])
        scratch = sb("scratch", [P, 1])
        eps = sb("eps", [P, 1])
        ones = sb("ones", [P, 1])
        dst_rows = start_only(SROWS, SCOLS * GROUP, I32).rearrange("p (k e) -> p k e", k=SCOLS)
        stat = sb("stat", [SROWS, 2, SCOLS])
        stat_b = start_only(SROWS, 2 * SCOLS * P).rearrange("p (w k m) -> p w k m", w=2, k=SCOLS)
        max_all = start_only(P, NSTAT)
        gidx = start_only(P, NSTAT)
        cend = sb("cend", [P, 1])
        need = sb("need", [P, 1])
        bend = start_only(P, BATCHES)
        span_i = start_only(1, NSTAT, I32)
        x_ln = edgeT[0:QUART, :].rearrange("p (t f) -> p t f", f=H)
        bn = start_only(QUART, CHUNKS * NQ * 6).rearrange("p (t s) -> p t s", s=6)
        mv = start_only(QUART, CHUNKS * NQ * 2).rearrange("p (t s) -> p t s", s=2)
        std = start_only(QUART, CHUNKS * NQ)
        rstd = start_only(QUART, CHUNKS * NQ)
        shift = start_only(QUART, CHUNKS * NQ)
        KEPT_EARLY = 11
        assert KEPT_EARLY * CHUNK <= room[0]
        CLEARED = KEPT_EARLY + 4
        m_sb = gru[:, 0 * CHUNK:1 * CHUNK]
        r_sb = gru[:, 1 * CHUNK:2 * CHUNK]
        z_sb = gru[:, 2 * CHUNK:3 * CHUNK]
        t_sb = r_sb
        zh_sb = m_sb
        n_sb = gru[:, 3 * CHUNK:4 * CHUNK]
        h_new = gru[:, 4 * CHUNK:5 * CHUNK]
        x_in = sb("x_in", [QUART, NQ, H])
        out_sb = sb("out_sb", [QUART, NQ, H])

        ps_win = [ctx.enter_context(nc.psum_tensor(f"ps_win{i}", [P, 512], F32)) for i in range(2)]
        ps_m = ctx.enter_context(nc.psum_tensor("ps_m", [P, 512], F32))
        ps_r = ctx.enter_context(nc.psum_tensor("ps_r", [P, 512], F32))
        ps_z = ctx.enter_context(nc.psum_tensor("ps_z", [P, 512], F32))
        ps_ni = ctx.enter_context(nc.psum_tensor("ps_ni", [P, 512], F32))
        ps_nh = ctx.enter_context(nc.psum_tensor("ps_nh", [P, 512], F32))
        ps_t = ctx.enter_context(nc.psum_tensor("ps_t", [P, 512], F32))

        idx_loaded = [sem(f"idx_loaded{s}") for s in range(RING)]
        attr_loaded = [sem(f"attr_loaded{s}") for s in range(RING)]
        rows_loaded = [sem(f"rows_loaded{s}") for s in range(RING)]
        gather_issued = sem("gather_issued")
        dst_rows_loaded = sem("dst_rows_loaded")
        w_loaded = sem("w_loaded")
        x_loaded = [sem(f"x_loaded{i}") for i in range(len(X_LOADS))]
        consts_made = sem("consts_made")
        ident_zeroed = sem("ident_zeroed")
        prep = sem("prep")
        stat_ready = sem("stat_ready")
        base_ps_ready = sem("base_ps_ready")
        need_ready = sem("need_ready")
        ready_ps_ready = sem("ready_ps_ready")
        tables_ready = sem("tables_ready")
        w_turned = sem("w_turned")
        w_kept = sem("w_kept")
        b_turned = sem("b_turned")
        bias_ready = sem("bias_ready")
        ln_stats = sem("ln_stats")
        ln_aggr = sem("ln_aggr")
        ln_std = sem("ln_std")
        ln_rstd = sem("ln_rstd")
        ln_shift = sem("ln_shift")
        ln_relu = sem("ln_relu")
        ln_turned = sem("ln_turned")
        agg_zeroed = sem("agg_zeroed")
        ln_kept = {"dve": sem("ln_kept_dve"), "act": sem("ln_kept_act")}
        h_stored = [sem("h_stored_low"), sem("h_stored_high")]
        sums_zeroed = sem("sums_zeroed")
        rel_ready = sem("rel_ready")
        onehot_ready = sem("onehot_ready")
        group_summed = sem("group_summed")
        window_added = sem("window_added")
        rel_x_ready = sem("rel_x_ready")
        x_onehot_ready = sem("x_onehot_ready")
        x_summed = sem("x_summed")
        x_added = sem("x_added")
        msg_ready = sem("msg_ready")
        m_kept = sem("m_kept")
        r_summed = sem("r_summed")
        n_summed = sem("n_summed")
        z_summed = sem("z_summed")
        r_ready = sem("r_ready")
        z_ready = sem("z_ready")
        t_scaled = sem("t_scaled")
        t_ready = sem("t_ready")
        n_ready = sem("n_ready")
        zh_ready = sem("zh_ready")
        zc_ready = sem("zc_ready")
        zn_ready = sem("zn_ready")
        h_ready = sem("h_ready")
        h_turned = sem("h_turned")
        hT_kept = sem("hT_kept")
        agg_cleared = sem("agg_cleared")
        x_in_loaded = sem("x_in_loaded")
        out_ready = sem("out_ready")
        out_stored = sem("out_stored")
        chunk_done = sem("chunk_done")

        LN_BANKS = (ps_t, ps_m, ps_ni, ps_nh)

        def keeper(c):
            if c < KEPT_EARLY:
                return "dve", c + 1
            n = (c - KEPT_EARLY) // 2 + 1
            return ("dve", KEPT_EARLY + n) if (c - KEPT_EARLY) % 2 else ("act", n)

        def kept_by(who):
            return [c for c in range(CHUNKS) if keeper(c)[0] == who]

        def slot_use(layer, b, s):
            return layer * (BATCHES + (s == 0)) + b

        def first_batch(group):
            for s in range(RING):
                group(0, s, s, P, True)

        def other_groups(eng, group):
            with eng.Fori(1, BATCHES) as b:
                for s in range(RING):
                    group(b, s, b * RING + s, P, False)
            group(BATCHES, 0, FULL, REST, False)

        def ready_chunks(eng, b, chunk):
            lo = eng.value_load(ready_i[0:1, bass.ds(b, 1)], min_val=0, max_val=CHUNKS)
            hi = eng.value_load(ready_i[0:1, bass.ds(b + 1, 1)], min_val=0, max_val=CHUNKS)
            with eng.If(lo < hi):
                with eng.Fori(lo, hi) as c:
                    chunk(c)

        def last_chunks(eng, chunk):
            lo = eng.value_load(ready_i[0:1, BATCHES:BATCHES + 1], min_val=0, max_val=CHUNKS)
            with eng.If(lo < CHUNKS):
                with eng.Fori(lo, CHUNKS) as c:
                    chunk(c)

        def edges(a, g, parts):
            w = a.shape[1] if len(a.shape) == 2 else 1
            flat = a if w == 1 else a.rearrange("e d -> (e d)")
            if parts == P:
                v = flat[0:FULL * GROUP * w].rearrange("(g p j) -> g p j", g=FULL, p=P)
                return v[bass.ds(g, 1), :, :].rearrange("o p j -> p (o j)")
            return flat[FULL * GROUP * w:E * w].rearrange("(p j) -> p j", p=parts)

        def nodes(a, c):
            v = a.rearrange("(c q p) f -> c p q f", q=NQ, p=QUART)
            return v[bass.ds(c, 1), :, :, :].rearrange("o p q f -> p (o q) f")

        def cols(t, c):
            return t[:, bass.ds(c * CHUNK, CHUNK)]

        ctx.enter_context(nc.allow_non_contiguous_dma("edge groups are 16 bytes to a partition"))
        block = ctx.enter_context(nc.Block())

        @block.sync
        def _(sp):
            xv = x.rearrange("(t p) f -> p t f", p=QUART)
            for c, n, loaded in zip(x_starts, X_LOADS, x_loaded):
                sp.dma_start(x_ln[:, c * NQ:(c + n) * NQ, :], xv[:, c * NQ:(c + n) * NQ, :]).then_inc(loaded, 16)
            head = (SCOLS - 1) * SROWS * GROUP
            sp.dma_start(dst_rows[:, 0:SCOLS - 1, :],
                         dst[0:head].rearrange("(k p j) -> p k j", p=SROWS, j=GROUP)).then_inc(dst_rows_loaded, 16)
            more = FULL - (SCOLS - 1) * SROWS
            sp.dma_start(dst_rows[0:more, SCOLS - 1, :],
                         dst[head:FULL * GROUP].rearrange("(p j) -> p j", j=GROUP)).then_inc(dst_rows_loaded, 16)
            for p in range(more, SROWS):
                sp.dma_start(dst_rows[p:p + 1, SCOLS - 1, :],
                             dst[E - GROUP:E].rearrange("(o j) -> o j", o=1)).then_inc(dst_rows_loaded, 16)
            for layer in range(2):
                w_msg, w_ih, w_hh, b_ih, b_hh = weights[layer]
                sp.dma_start(w_raw[:, layer, 0, :], w_msg[:, 0:H]).then_inc(w_loaded, 16)
                sp.dma_start(w_raw[:, layer, 1, 0:D], w_msg[:, H:H + D]).then_inc(w_loaded, 16)
                sp.dma_start(w_raw[:, layer, 2:5, :], w_ih.rearrange("(t p) k -> p t k", p=P)).then_inc(w_loaded, 16)
                sp.dma_start(w_raw[:, layer, 5:8, :], w_hh.rearrange("(t p) k -> p t k", p=P)).then_inc(w_loaded, 16)
                for k, b in enumerate((b_ih, b_hh)):
                    o = 6 * layer + 3 * k
                    sp.dma_start(b_raw[o:o + 3, :], b.rearrange("(t p) -> t p", p=P)).then_inc(w_loaded, 16)

            for layer in range(2):
                def group(b, s, g, parts, first):
                    again = layer or not first
                    if again:
                        sp.wait_ge(rows_loaded[s], slot_use(layer, b, s) * 16 * TILES)
                    sp.dma_start(idx[0:parts, s, :], edges(src, g, parts)).then_inc(idx_loaded[s], 16)
                    if layer == 0:
                        if again:
                            sp.wait_ge(group_summed, g - RING + 1)
                        sp.dma_start(dst_in[0:parts, s, :], edges(dst, g, parts)).then_inc(attr_loaded[s], 16)
                        sp.dma_start(attr[0:parts, s, :, :].rearrange("p j d -> p (j d)"),
                                     edges(edge_attr, g, parts)).then_inc(attr_loaded[s], 16)

                first_batch(group)
                if layer == 0:
                    for c in range(CHUNKS):
                        sp.wait_ge(ln_relu, c + 1)
                        sp.dma_start(nodes(h_table, c), x_ln[:, c * NQ:(c + 1) * NQ, :]).then_inc(h_stored[c >= CLEARED], 16)
                other_groups(sp, group)

        @block.gpsimd
        def _(pool):
            nc.gpsimd.memset(ident[:, :], 0.0).then_inc(ident_zeroed, 1)
            small = {"allow_small_or_imprecise_dtypes": True}
            nc.gpsimd.iota(lane[:, :], pattern=[[1, XWIN]], base=0, channel_multiplier=0, **small)
            nc.gpsimd.iota(gidx[:, :], pattern=[[1, NSTAT]], base=1, channel_multiplier=0, **small)
            nc.gpsimd.iota(cend[:, :], pattern=[[1, 1]], base=CHUNK, channel_multiplier=CHUNK, **small)
            nc.gpsimd.iota(bend[:, :], pattern=[[RING, BATCHES]], base=RING, channel_multiplier=0, **small)
            nc.gpsimd.memset(zero[:, :], 0.0)
            nc.gpsimd.memset(eps[:, :], EPS)
            nc.gpsimd.memset(ones[:, :], 1.0)
            pool.wait_ge(ident_zeroed, 1)
            nc.gpsimd.affine_select(out=ident[:, :], in_=ident[:, :], compare_op=ALU.not_equal, fill=1.0, base=0,
                                    pattern=[[-1, P]], channel_multiplier=1).then_inc(consts_made, 1)
            nc.gpsimd.memset(aggT[:, :], 0.0)
            pool.wait_ge(ln_turned, CLEARED)
            pool.wait_ge(h_stored[0], 16 * CLEARED)
            nc.gpsimd.memset(edgeT[0:D, 0:CLEARED * NQ * H], 0.0).then_inc(agg_zeroed, 1)

            for layer in range(2):
                table = (h_table, x1_table)[layer]
                if layer == 0:
                    pool.wait_ge(h_stored[1], 16 * (CHUNKS - CLEARED))
                else:
                    pool.wait_ge(out_stored, 16 * CHUNKS)

                def group(b, s, g, parts, first):
                    if layer or not first:
                        pool.wait_ge(group_summed, layer * GROUPS + g - RING + 1)
                    pool.wait_ge(idx_loaded[s], 16 * (slot_use(layer, b, s) + 1))
                    pool.sem_inc(gather_issued, 1)
                    for j in range(TILES):
                        nc.gpsimd.indirect_dma_start(
                            out=rows[0:parts, s, j, :], out_offset=None, in_=table[:, :],
                            in_offset=bass.IndirectOffsetOnAxis(ap=idx[0:parts, s, j:j + 1].bitcast(U32), axis=0),
                        ).then_inc(rows_loaded[s], 16)

                first_batch(group)
                other_groups(pool, group)

        @block.tensor
        def _(pe):
            pe.wait_ge(consts_made, 1)
            def turn_nodes(c):
                pe.wait_ge(ln_relu, c + 1)
                if c >= len(LN_BANKS):
                    who, count = keeper(c - len(LN_BANKS))
                    pe.wait_ge(ln_kept[who], count)
                for q in range(NQ):
                    tr = nc.tensor.transpose(LN_BANKS[c % len(LN_BANKS)][:, q * QUART:(q + 1) * QUART],
                                             x_ln[:, c * NQ + q, :], ident[0:QUART, 0:QUART])
                tr.then_inc(ln_turned, 1)

            for c in range(KEPT_EARLY + len(LN_BANKS)):
                turn_nodes(c)
            pe.wait_ge(stat_ready, 1)
            for w, ps in ((0, ps_r), (1, ps_z)):
                for k in range(SCOLS):
                    mm = nc.tensor.matmul(ps[:, k * SROWS:(k + 1) * SROWS], stat_b[:, w, k, :],
                                          ident[0:SROWS, 0:SROWS], start=True, stop=True)
            mm.then_inc(base_ps_ready, 1)
            pe.wait_ge(w_loaded, 16 * 12)
            nc.tensor.transpose(ps_win[1][:, 0:12], b_raw[:, :], ident[0:12, 0:12]).then_inc(b_turned, 1)
            pe.wait_ge(need_ready, 1)
            nc.tensor.matmul(ps_win[0][0:1, 0:BATCHES], ones[0:CHUNKS, :], bend[0:CHUNKS, :],
                             start=True, stop=True).then_inc(ready_ps_ready, 1)

            pe.wait_ge(tables_ready, 1)
            for c in range(KEPT_EARLY + len(LN_BANKS), CHUNKS):
                turn_nodes(c)
            for layer in range(2):
                for k in range(8):
                    i = layer * 8 + k
                    bank = ps_win[i % 2]
                    if i == 0:
                        pe.wait_ge(tables_ready, 1)
                    if i == 1:
                        pe.wait_ge(bias_ready, 1)
                    if i >= 2:
                        pe.wait_ge(w_kept, i - 1)
                    part = D if k == 1 else P
                    nc.tensor.transpose(bank[0:part, 0:P], w_raw[:, layer, k, 0:part], ident[:, :]).then_inc(w_turned, 1)
            pe.wait_ge(w_kept, 16)
            for who in ("dve", "act"):
                pe.wait_ge(ln_kept[who], len(kept_by(who)))
            extra_count = pe.alloc_register("pe_extra_count")
            pe.reg_mov(extra_count, 0)

            for layer in range(2):
                def group(b, s, g, parts):
                    gg = layer * GROUPS + g
                    bank = ps_win[s % 2]
                    n = pe.value_load(extra_i[0:1, bass.ds(g, 1)], min_val=0, max_val=N)
                    if layer == 0:
                        pe.wait_ge(attr_loaded[s], 32 * (slot_use(0, b, s) + 1))
                    pe.wait_ge(onehot_ready, gg + 1)
                    if layer == 0:
                        for j in range(TILES):
                            nc.tensor.matmul(bank[0:D, WIN:2 * WIN], attr[0:parts, s, j, :],
                                             onehot[0:parts, s % 2, j, :], start=(j == 0), stop=(j == TILES - 1))
                    pe.wait_ge(rows_loaded[s], 16 * TILES * (slot_use(layer, b, s) + 1))
                    with pe.If(n > 0):
                        with pe.Fori(0, n):
                            pe.reg_add(extra_count, extra_count, 1)
                            count = pe.snap(extra_count, min_val=1, max_val=1 << 20)
                            pe.wait_ge(x_onehot_ready, count)
                            for j in range(TILES):
                                mm = nc.tensor.matmul(bank[:, XAT:XAT + XWIN], rows[0:parts, s, j, :],
                                                      onehot_x[0:parts, j, :], start=(j == 0), stop=(j == TILES - 1))
                            if layer == 0:
                                for j in range(TILES):
                                    mm = nc.tensor.matmul(bank[0:D, XAT + XWIN:XAT + 2 * XWIN],
                                                          attr[0:parts, s, j, :], onehot_x[0:parts, j, :],
                                                          start=(j == 0), stop=(j == TILES - 1))
                            mm.then_inc(x_summed, 1)
                            pe.wait_ge(x_added, count)
                    for j in range(TILES):
                        mm = nc.tensor.matmul(bank[:, 0:WIN], rows[0:parts, s, j, :],
                                              onehot[0:parts, s % 2, j, :], start=(j == 0), stop=(j == TILES - 1))
                    mm.then_inc(group_summed, 1)

                def turn_back(cc):
                    pe.wait_ge(h_ready, cc)
                    pe.wait_ge(chunk_done, cc)
                    for q in range(NQ):
                        tr = nc.tensor.transpose(ps_t[0:QUART, q * P:(q + 1) * P],
                                                 h_new[:, q * QUART:(q + 1) * QUART], ident[:, :])
                    tr.then_inc(h_turned, 1)

                def chunk(c, groups_done):
                    cc = layer * CHUNKS + c
                    with pe.If(c > 0):
                        turn_back(cc)
                    nc.tensor.matmul(ps_r[:, 0:CHUNK], wT[:, layer, 5, :], cols(hT, c), start=True, stop=False)
                    pe.wait_ge(window_added, layer * GROUPS + groups_done)
                    nc.tensor.matmul(ps_m[:, 0:CHUNK], wT[:, layer, 0, :], cols(aggT, c), start=True, stop=False)
                    nc.tensor.matmul(ps_m[:, 0:CHUNK], wT[0:D, layer, 1, :], cols(edgeT[0:D, :], c),
                                     start=False, stop=True).then_inc(msg_ready, 1)
                    nc.tensor.matmul(ps_nh[:, 0:CHUNK], wT[:, layer, 7, :], cols(hT, c), start=True, stop=True)
                    pe.wait_ge(m_kept, cc + 1)
                    nc.tensor.matmul(ps_r[:, 0:CHUNK], wT[:, layer, 2, :], m_sb[:, :],
                                     start=False, stop=True).then_inc(r_summed, 1)
                    nc.tensor.matmul(ps_ni[:, 0:CHUNK], wT[:, layer, 4, :], m_sb[:, :],
                                     start=True, stop=True).then_inc(n_summed, 1)
                    nc.tensor.matmul(ps_z[:, 0:CHUNK], wT[:, layer, 6, :], cols(hT, c), start=True, stop=False)
                    nc.tensor.matmul(ps_z[:, 0:CHUNK], wT[:, layer, 3, :], m_sb[:, :],
                                     start=False, stop=True).then_inc(z_summed, 1)

                if layer == 1:
                    pe.wait_ge(hT_kept, CHUNKS)
                with pe.Fori(0, BATCHES) as b:
                    for s in range(RING):
                        group(b, s, b * RING + s, P)
                    ready_chunks(pe, b, lambda c: chunk(c, (b + 1) * RING))
                group(BATCHES, 0, FULL, REST)
                last_chunks(pe, lambda c: chunk(c, GROUPS))
                turn_back((layer + 1) * CHUNKS)

        @block.vector
        def _(dve):
            step = [0]

            def chained(ins):
                step[0] += 1
                ins.then_inc(prep, 1)
                dve.wait_ge(prep, step[0])

            def keep_nodes(c):
                dve.wait_ge(ln_turned, c + 1)
                nc.vector.tensor_copy(hT[:, c * CHUNK:(c + 1) * CHUNK],
                                      LN_BANKS[c % len(LN_BANKS)][:, 0:CHUNK]).then_inc(ln_kept["dve"], 1)

            for c in range(CHUNKS + 1):
                if c < CHUNKS:
                    if c in x_starts:
                        dve.wait_ge(x_loaded[x_starts.index(c)], 16)
                    for t in range(c * NQ, (c + 1) * NQ):
                        ins = nc.vector.bn_stats(bn[:, t, :], x_ln[:, t, :])
                    ins.then_inc(ln_stats, 1)
                if c >= 1:
                    dve.wait_ge(ln_std, c)
                    last = slice((c - 1) * NQ, c * NQ)
                    nc.vector.reciprocal(rstd[:, last], std[:, last]).then_inc(ln_rstd, 1)
                if c < CHUNKS:
                    dve.wait_ge(ln_stats, c + 1)
                    for t in range(c * NQ, (c + 1) * NQ):
                        ins = nc.vector.bn_aggr(mv[:, t, :], bn[:, t, :])
                    ins.then_inc(ln_aggr, 1)
                if c >= 1:
                    dve.wait_ge(ln_rstd, c)
                    nc.vector.scalar_tensor_tensor(out=shift[:, last], in0=mv[:, last, 0], scalar=-1.0, in1=rstd[:, last],
                                                   op0=ALU.mult, op1=ALU.mult).then_inc(ln_shift, 1)
                if c >= 4 and c % 2 == 0:
                    keep_nodes((c - 4) // 2)
            assert (CHUNKS - 1 - 4) // 2 + 1 == KEPT_EARLY

            dve.wait_ge(dst_rows_loaded, 16 * (2 + SROWS - (FULL - (SCOLS - 1) * SROWS)))
            nc.vector.tensor_reduce(stat[:, 0, :], dst_rows[:, :, :], AX.X, ALU.min)
            chained(nc.vector.tensor_reduce(stat[:, 1, :], dst_rows[:, :, :], AX.X, ALU.max))
            chained(nc.vector.tensor_scalar(stat[:, :, :], stat[:, :, :], 0.0, float(N), ALU.max, ALU.min))
            nc.vector.tensor_copy(stat_b[:, :, :, :],
                                  stat[:, :, :].unsqueeze(3).to_broadcast([SROWS, 2, SCOLS, P])).then_inc(stat_ready, 1)
            dve.wait_ge(base_ps_ready, 1)
            nc.vector.tensor_copy(base_all[:, :], ps_r[:, 0:NSTAT])
            chained(nc.vector.tensor_copy(max_all[:, :], ps_z[:, 0:NSTAT]))
            nc.vector.tensor_copy(base_i[:, :], base_all[0:1, :])
            chained(nc.vector.tensor_tensor(max_all[0:1, :], max_all[0:1, :], base_all[0:1, :], ALU.subtract))
            chained(nc.vector.tensor_scalar(span_i[:, :], max_all[0:1, :], float(XWIN - WIN), None, ALU.add))
            nc.vector.tensor_scalar(extra_i[:, :], span_i[:, :], XSHIFT, None, ALU.arith_shift_right)
            chained(nc.vector.scalar_tensor_tensor(out=gidx[:, :], in0=base_all[:, :], scalar=cend[:, 0:1],
                                                   in1=gidx[:, :], op0=ALU.is_lt, op1=ALU.mult))
            chained(nc.vector.tensor_reduce(need[:, :], gidx[:, :], AX.X, ALU.max))
            nc.vector.tensor_scalar(bend[:, :], bend[:, :], need[:, 0:1], None, ALU.is_ge).then_inc(need_ready, 1)
            nc.vector.memset(ready_i[0:1, 0:1], 0)
            dve.wait_ge(ready_ps_ready, 1)
            nc.vector.tensor_copy(ready_i[0:1, 1:BATCHES + 1], ps_win[0][0:1, 0:BATCHES]).then_inc(tables_ready, 1)

            dve.wait_ge(b_turned, 1)
            chained(nc.vector.tensor_copy(bT[:, :], ps_win[1][:, 0:12]))
            for layer in range(2):
                o = 6 * layer
                ins = nc.vector.tensor_tensor(b_gate[:, layer, :], bT[:, o:o + 2], bT[:, o + 3:o + 5], ALU.add)
            ins.then_inc(bias_ready, 1)

            dve.wait_ge(ln_relu, CHUNKS)
            for c in kept_by("dve")[KEPT_EARLY:]:
                keep_nodes(c)
            dve.wait_ge(ln_turned, CHUNKS)
            dve.wait_ge(h_stored[1], 16 * (CHUNKS - CLEARED))
            dve.wait_ge(agg_zeroed, 1)
            nc.vector.memset(edgeT[0:D, CLEARED * NQ * H:COLS], 0.0).then_inc(sums_zeroed, 1)
            dve.wait_ge(sums_zeroed, 1)

            extra_count = dve.alloc_register("dve_extra_count")
            dve.reg_mov(extra_count, 0)

            for layer in range(2):
                def relative(g, parts):
                    return dst_rel[0:parts, bass.ds(g, 1), :].rearrange("p o j -> p (o j)")

                def onehot_of(b, s, g):
                    rel = relative(g, P)
                    if layer == 0:
                        dve.wait_ge(attr_loaded[s], 32 * (slot_use(0, b, s) + 1))
                        nc.vector.tensor_scalar(rel, dst_in[:, s, :], float(N), base_all[:, bass.ds(g, 1)],
                                                ALU.min, ALU.subtract).then_inc(rel_ready, 1)
                        dve.wait_ge(rel_ready, g + 1)
                    nc.vector.tensor_tensor(
                        onehot[:, s % 2, :, :],
                        lane[:, 0:WIN].unsqueeze(1).to_broadcast([P, TILES, WIN]),
                        rel.unsqueeze(2).to_broadcast([P, TILES, WIN]), ALU.is_equal).then_inc(onehot_ready, 1)

                def extra_windows(s, g, parts, base):
                    n = dve.value_load(extra_i[0:1, bass.ds(g, 1)], min_val=0, max_val=N)
                    with dve.If(n > 0):
                        nc.vector.tensor_scalar(rel_x[0:parts, :], relative(g, parts), float(WIN), None,
                                                ALU.subtract).then_inc(rel_x_ready, 1)
                        with dve.Fori(0, n) as k:
                            dve.reg_add(extra_count, extra_count, 1)
                            count = dve.snap(extra_count, min_val=1, max_val=1 << 20)
                            dve.drain()
                            nc.vector.tensor_tensor(
                                onehot_x[0:parts, :, :],
                                lane[0:parts, :].unsqueeze(1).to_broadcast([parts, TILES, XWIN]),
                                rel_x[0:parts, :].unsqueeze(2).to_broadcast([parts, TILES, XWIN]),
                                ALU.is_equal).then_inc(x_onehot_ready, 1)
                            dve.wait_ge(x_summed, count)
                            nc.vector.tensor_scalar(rel_x[0:parts, :], rel_x[0:parts, :], float(XWIN), None,
                                                    ALU.subtract)
                            at = base + k * XWIN + WIN
                            at = nc.s_assert_within(
                                at, WIN, COLS - XWIN,
                                skip_runtime_bounds_check_because="an extra window starts at or before the group's greatest node")
                            if layer == 0:
                                e = edgeT[0:D, bass.ds(at, XWIN)]
                                nc.vector.tensor_tensor(e, e, ps_win[s % 2][0:D, XAT + XWIN:XAT + 2 * XWIN], ALU.add)
                            a = aggT[:, bass.ds(at, XWIN)]
                            nc.vector.tensor_tensor(a, a, ps_win[s % 2][:, XAT:XAT + XWIN], ALU.add).then_inc(x_added, 1)
                            dve.wait_ge(x_added, count)

                def add_window(s, g, parts):
                    base = dve.value_load(base_i[0:1, bass.ds(g, 1)], min_val=0, max_val=N)
                    extra_windows(s, g, parts, base)
                    dve.wait_ge(group_summed, layer * GROUPS + g + 1)
                    if layer == 0:
                        e = edgeT[0:D, bass.ds(base, WIN)]
                        nc.vector.tensor_tensor(e, e, ps_win[s % 2][0:D, WIN:2 * WIN], ALU.add)
                    a = aggT[:, bass.ds(base, WIN)]
                    nc.vector.tensor_tensor(a, a, ps_win[s % 2][:, 0:WIN], ALU.add).then_inc(window_added, 1)

                def batch(b, last):
                    for s in range(RING):
                        g = b * RING + s
                        add_window(s, g, P)
                        if not (last and s == RING - 1):
                            onehot_of(b + (s + 2) // RING, (s + 2) % RING, g + 2)
                        dve.wait_ge(window_added, layer * GROUPS + g + 1)
                    ready_chunks(dve, b, chunk)

                def add_nodes(cc):
                    dve.wait_ge(h_turned, cc)
                    dve.wait_ge(x_in_loaded, 16 * (cc - CHUNKS))
                    dve.wait_ge(chunk_done, cc)
                    nc.vector.tensor_tensor(
                        out_sb[:, :, :], x_in[:, :, :],
                        ps_t[0:QUART, 0:NQ * H].rearrange("p (q f) -> p q f", f=H), ALU.add).then_inc(out_ready, 1)

                def chunk(c):
                    cc = layer * CHUNKS + c
                    o = 6 * layer
                    if layer == 1:
                        with dve.If(c > 0):
                            add_nodes(cc)
                    dve.wait_ge(n_summed, cc + 1)
                    dve.wait_ge(r_ready, cc + 1)
                    nc.vector.scalar_tensor_tensor(out=t_sb[:, :], in0=ps_nh[:, 0:CHUNK], scalar=bT[:, o + 5:o + 6],
                                                   in1=r_sb[:, :], op0=ALU.add, op1=ALU.mult).then_inc(t_scaled, 1)
                    dve.wait_ge(t_scaled, cc + 1)
                    nc.vector.tensor_tensor(t_sb[:, :], t_sb[:, :], ps_ni[:, 0:CHUNK], ALU.add).then_inc(t_ready, 1)
                    dve.wait_ge(z_ready, cc + 1)
                    nc.vector.tensor_tensor(zh_sb[:, :], z_sb[:, :], cols(hT, c), ALU.mult).then_inc(zh_ready, 1)
                    dve.wait_ge(zh_ready, cc + 1)
                    nc.vector.tensor_scalar(z_sb[:, :], z_sb[:, :], -1.0, 1.0, ALU.mult, ALU.add).then_inc(zc_ready, 1)
                    dve.wait_ge(n_ready, cc + 1)
                    dve.wait_ge(zc_ready, cc + 1)
                    nc.vector.tensor_tensor(n_sb[:, :], n_sb[:, :], z_sb[:, :], ALU.mult).then_inc(zn_ready, 1)
                    dve.wait_ge(zn_ready, cc + 1)
                    nc.vector.tensor_tensor(h_new[:, :], n_sb[:, :], zh_sb[:, :], ALU.add).then_inc(h_ready, 1)

                onehot_of(0, 0, 0)
                onehot_of(0, 1, 1)
                if layer == 1:
                    dve.wait_ge(agg_cleared, CHUNKS)
                with dve.Fori(0, BATCHES - 1) as b:
                    batch(b, False)
                batch(BATCHES - 1, True)
                add_window(0, FULL, REST)
                last_chunks(dve, chunk)
                if layer == 1:
                    add_nodes(2 * CHUNKS)

        @block.scalar
        def _(act):
            act.sem_inc(chunk_done, 1)
            act.wait_ge(consts_made, 1)
            for i in range(CHUNKS + 2):
                if i < CHUNKS:
                    act.wait_ge(ln_aggr, i + 1)
                    nc.scalar.activation(std[:, i * NQ:(i + 1) * NQ], mv[:, i * NQ:(i + 1) * NQ, 1], ACT.Sqrt,
                                         bias=eps[0:QUART, :]).then_inc(ln_std, 1)
                if i >= 2:
                    c = i - 2
                    act.wait_ge(ln_shift, c + 1)
                    for t in range(c * NQ, (c + 1) * NQ):
                        ins = nc.scalar.activation(x_ln[:, t, :], x_ln[:, t, :], ACT.Relu,
                                                   bias=shift[:, t:t + 1], scale=rstd[:, t:t + 1])
                    ins.then_inc(ln_relu, 1)
            act.wait_ge(tables_ready, 1)
            act.wait_ge(bias_ready, 1)
            for c in kept_by("act"):
                act.wait_ge(ln_turned, c + 1)
                nc.scalar.copy(hT[:, c * CHUNK:(c + 1) * CHUNK],
                               LN_BANKS[c % len(LN_BANKS)][:, 0:CHUNK]).then_inc(ln_kept["act"], 1)
            for i in range(16):
                layer, k = i // 8, i % 8
                part = D if k == 1 else P
                act.wait_ge(w_turned, i + 1)
                nc.scalar.copy(wT[0:part, layer, k, :], ps_win[i % 2][0:part, 0:P]).then_inc(w_kept, 1)

            for layer in range(2):
                def nodes_out(c):
                    cc = layer * CHUNKS + c
                    if layer == 0:
                        act.wait_ge(h_turned, cc)
                        nc.scalar.copy(out_sb[:, :, :].rearrange("p q f -> p (q f)"),
                                       ps_t[0:QUART, 0:NQ * H]).then_inc(out_ready, 1)
                    act.wait_ge(out_ready, cc)
                    act.dma_start(nodes((x1_table, out)[layer], c - 1), out_sb[:, :, :]).then_inc(out_stored, 16)

                def nodes_stored(c):
                    act.wait_ge(out_stored, 16 * (layer * CHUNKS + c))
                    act.sem_inc(chunk_done, 1)

                def past_first(c):
                    return nc.s_assert_within(c, 1, CHUNKS - 1, skip_runtime_bounds_check_because="it is under c > 0")

                def chunk(c):
                    cc = layer * CHUNKS + c
                    o = 6 * layer
                    nc.scalar.activation(scratch[:, :], zero[:, :], ACT.Sigmoid)
                    with act.If(c > 0):
                        nodes_out(past_first(c))
                    if layer == 1:
                        act.dma_start(x_in[:, :, :], nodes(x, c)).then_inc(x_in_loaded, 16)
                    if layer == 1:
                        act.wait_ge(h_ready, cc)
                    act.wait_ge(msg_ready, cc + 1)
                    nc.scalar.copy(m_sb[:, :], ps_m[:, 0:CHUNK]).then_inc(m_kept, 1)
                    act.wait_ge(r_summed, cc + 1)
                    nc.scalar.activation(r_sb[:, :], ps_r[:, 0:CHUNK], ACT.Sigmoid,
                                         bias=b_gate[:, layer, 0:1]).then_inc(r_ready, 1)
                    act.wait_ge(z_summed, cc + 1)
                    nc.scalar.activation(z_sb[:, :], ps_z[:, 0:CHUNK], ACT.Sigmoid,
                                         bias=b_gate[:, layer, 1:2]).then_inc(z_ready, 1)
                    if layer == 0:
                        nc.scalar.copy(cols(aggT, c), zero[:, 0:1].to_broadcast([P, CHUNK])).then_inc(agg_cleared, 1)
                    act.wait_ge(t_ready, cc + 1)
                    nc.scalar.activation(n_sb[:, :], t_sb[:, :], ACT.Tanh, bias=bT[:, o + 2:o + 3]).then_inc(n_ready, 1)
                    if layer == 0:
                        act.wait_ge(h_ready, cc + 1)
                        nc.scalar.copy(cols(hT, c), h_new[:, :]).then_inc(hT_kept, 1)
                    with act.If(c > 0):
                        nodes_stored(past_first(c))

                with act.Fori(0, BATCHES) as b:
                    ready_chunks(act, b, chunk)
                last_chunks(act, chunk)
                nodes_out(CHUNKS)
                nodes_stored(CHUNKS)


_WEIGHTS = ["W_msg", "Wih", "Whh", "bih", "bhh"]


def kernel(**inputs):
    import numpy as _np
    import concourse.bacc as _bacc
    from concourse import mybir as _mybir
    from concourse.bass_utils import run_bass_kernel_spmd as _run

    nc = _bacc.Bacc("TRN2", target_bir_lowering=False, num_devices=1)
    arrays, aps = {}, {}
    names = ["x", "src", "dst", "edge_attr_64"] + [f"L0_gnn_{w}{n}" for n in (1, 2) for w in _WEIGHTS]
    for name in names:
        a = _np.ascontiguousarray(inputs[name])
        arrays[f"in_{name}_dram"] = a
        aps[name] = nc.dram_tensor(f"in_{name}_dram", a.shape, _mybir.dt.from_np(a.dtype), kind="ExternalInput").ap()
    shape = arrays["in_x_dram"].shape
    h_table = nc.dram_tensor("h_table", shape, F32, kind="Internal").ap()
    x1_table = nc.dram_tensor("x1_table", shape, F32, kind="Internal").ap()
    out = nc.dram_tensor("out_dram", shape, F32, kind="ExternalOutput").ap()
    weights = [[aps[f"L0_gnn_{w}{n}"] for w in _WEIGHTS] for n in (1, 2)]
    build(nc, aps["x"], aps["src"], aps["dst"], aps["edge_attr_64"], weights, h_table, x1_table, out)
    r = _run(nc, [arrays], core_ids=[0])
    return r.results[0]["out_dram"]
```
